# Optimizing a Trainium2 kernel written in Bass

```python
import numpy as np
import jax
import jax.numpy as jnp

def _softmax(x, axis=-1):
    return jax.nn.softmax(x, axis=axis)
def _gelu(x):
    return jax.nn.gelu(x, approximate=True)
def _silu(x):
    return jax.nn.silu(x)
def _sigmoid(x):
    return jax.nn.sigmoid(x)
def _layernorm(x, axis=-1, eps=1e-5):
    m = jnp.mean(x, axis=axis, keepdims=True)
    v = jnp.var(x, axis=axis, keepdims=True)
    return (x - m) / jnp.sqrt(v + eps)
def _scatter_add(tgt, idx, src, axis=0):
    return tgt.at[idx].add(src)
def _segment_sum(src, seg, n):
    return jax.ops.segment_sum(src, seg, n)

kernel_name = 'mk_conv_preact_d2_conv_nhwc256_836ebb'

def setup_inputs(seed: int = 0):
    np.random.seed(seed)
    _w = jnp.asarray
    def _rec_inputs():
        import jax
        import jax.numpy as jnp
        _gk = jax.random.key(seed)
        x = 7.22e-05 + 1 * jax.random.normal(jax.random.fold_in(_gk, 1), (1, 128, 256, 256), jnp.float32)
        return x
    x = _rec_inputs()
    def _L0_conv_setup():
        import jax, jax.numpy as jnp
        import numpy as np
        QKV_DIM = 256
        C = 32
        N_HEAD = 8
        OUT_DIM = 256
        key = jax.random.key(seed)
        ks = jax.random.split(key, 9)
        hc = N_HEAD * C
        in_data = jax.random.normal(ks[0], (1, 128, 256, QKV_DIM), dtype=jnp.float32)
        nonbatched_bias = jax.random.normal(ks[1], (1, N_HEAD, 256, 256), dtype=jnp.float32)
        s = 1.0 / np.sqrt(QKV_DIM)
        Wq = jax.random.normal(ks[2], (hc, QKV_DIM), dtype=jnp.float32) * s
        Wk = jax.random.normal(ks[3], (hc, QKV_DIM), dtype=jnp.float32) * s
        Wv = jax.random.normal(ks[4], (hc, QKV_DIM), dtype=jnp.float32) * s
        Wg = jax.random.normal(ks[5], (hc, QKV_DIM), dtype=jnp.float32) * 0.02
        gating_bias = jnp.ones((hc,), dtype=jnp.float32)
        Wo = jax.random.normal(ks[6], (OUT_DIM, hc), dtype=jnp.float32) * 0.02
        bo = jnp.zeros((OUT_DIM,), dtype=jnp.float32)
        return {'in_data': in_data, 'nonbatched_bias': nonbatched_bias, 'Wq': Wq, 'Wk': Wk, 'Wv': Wv, 'Wg': Wg, 'gating_bias': gating_bias, 'Wo': Wo, 'bo': bo}
    _L0_conv_all = _L0_conv_setup()
    _L0_conv_in = {k: v for k, v in _L0_conv_all.items() if k in ('nonbatched_bias', 'Wq', 'Wk', 'Wv', 'Wg', 'gating_bias', 'Wo', 'bo', )}
    del _L0_conv_all

    def _L1_conv_setup():
        import jax, jax.numpy as jnp
        import numpy as np
        QKV_DIM = 256
        C = 32
        N_HEAD = 8
        OUT_DIM = 256
        B1, B2, N = (1, 128, 256)
        key = jax.random.key(seed)
        ks = jax.random.split(key, 8)
        hc = N_HEAD * C
        return {'in_data': jax.random.normal(ks[0], (B1, B2, N, QKV_DIM), jnp.float32), 'mask': jnp.ones((B1, B2, N), jnp.float32), 'nonbatched_bias': jax.random.normal(ks[1], (B1, N_HEAD, N, N), jnp.float32), 'w_qkv': jax.random.normal(ks[2], (3 * hc, QKV_DIM), jnp.float32) * (1.0 / np.sqrt(QKV_DIM)), 'w_gate': jax.random.normal(ks[3], (hc, QKV_DIM), jnp.float32) * 0.02, 'gating_bias': jnp.ones((hc,), jnp.float32), 'w_o': jax.random.normal(ks[4], (OUT_DIM, hc), jnp.float32) * 0.02, 'b_o': jnp.zeros((OUT_DIM,), jnp.float32)}
    _L1_conv_all = _L1_conv_setup()
    _L1_conv_in = {k: v for k, v in _L1_conv_all.items() if k in ('mask', 'nonbatched_bias', 'w_qkv', 'w_gate', 'gating_bias', 'w_o', 'b_o', )}
    del _L1_conv_all

    return {
        "x": x,
        "L0_conv_nonbatched_bias": _L0_conv_in["nonbatched_bias"],
        "L0_conv_Wq": _L0_conv_in["Wq"],
        "L0_conv_Wk": _L0_conv_in["Wk"],
        "L0_conv_Wv": _L0_conv_in["Wv"],
        "L0_conv_Wg": _L0_conv_in["Wg"],
        "L0_conv_gating_bias": _L0_conv_in["gating_bias"],
        "L0_conv_Wo": _L0_conv_in["Wo"],
        "L0_conv_bo": _L0_conv_in["bo"],
        "L1_conv_mask": _L1_conv_in["mask"],
        "L1_conv_nonbatched_bias": _L1_conv_in["nonbatched_bias"],
        "L1_conv_w_qkv": _L1_conv_in["w_qkv"],
        "L1_conv_w_gate": _L1_conv_in["w_gate"],
        "L1_conv_gating_bias": _L1_conv_in["gating_bias"],
        "L1_conv_w_o": _L1_conv_in["w_o"],
        "L1_conv_b_o": _L1_conv_in["b_o"],
    }

def reference(x, L0_conv_nonbatched_bias, L0_conv_Wq, L0_conv_Wk, L0_conv_Wv, L0_conv_Wg, L0_conv_gating_bias, L0_conv_Wo, L0_conv_bo, L1_conv_mask, L1_conv_nonbatched_bias, L1_conv_w_qkv, L1_conv_w_gate, L1_conv_gating_bias, L1_conv_w_o, L1_conv_b_o):
    import jax
    import jax.numpy as jnp
    def _L0_conv_ref(in_data, nonbatched_bias, Wq, Wk, Wv, Wg, gating_bias, Wo, bo):
        import jax, jax.numpy as jnp
        import numpy as np
        QKV_DIM = 256
        C = 32
        N_HEAD = 8
        OUT_DIM = 256
        scaling = C ** (-0.5)

        def proj(W):
            y = jnp.einsum('abld,ed->able', in_data, W)
            b1, b2, L, _ = y.shape
            return y.reshape(b1, b2, L, N_HEAD, C).transpose(0, 1, 3, 2, 4)
        q = proj(Wq) * scaling
        k = proj(Wk)
        v = proj(Wv)
        logits = jnp.einsum('abhqc,abhkc->abhqk', q, k)
        logits = logits + nonbatched_bias[:, None]
        weights = jax.nn.softmax(logits, axis=-1)
        wavg = jnp.einsum('abhqk,abhkc->abhqc', weights, v)
        b1, b2, H, L, c = wavg.shape
        wavg = wavg.transpose(0, 1, 3, 2, 4).reshape(b1, b2, L, H * c)
        gate = jax.nn.sigmoid(jnp.einsum('abld,ed->able', in_data, Wg) + gating_bias)
        wavg = gate * wavg
        out = jnp.einsum('able,oe->ablo', wavg, Wo) + bo
        return out

    def _L1_conv_ref(in_data, mask, nonbatched_bias, w_qkv, w_gate, gating_bias, w_o, b_o):
        import jax, jax.numpy as jnp
        import numpy as np
        QKV_DIM = 256
        C = 32
        N_HEAD = 8
        OUT_DIM = 256
        B1, B2, N = (1, 128, 256)
        scaling = C ** (-0.5)
        qkv = jnp.einsum('abnd,ed->abne', in_data, w_qkv)
        q, k, v = jnp.split(qkv, 3, axis=-1)

        def to_heads(t):
            b1, b2, n, _ = t.shape
            return t.reshape(b1, b2, n, N_HEAD, C).transpose(0, 1, 3, 2, 4)
        q, k, v = (to_heads(q) * scaling, to_heads(k), to_heads(v))
        logits = jnp.einsum('abhqd,abhkd->abhqk', q, k)
        mask_bias = (mask[:, :, None, None, :] - 1.0) * 1000000000.0
        logits = logits + mask_bias + nonbatched_bias[:, None]
        weights = jax.nn.softmax(logits, axis=-1)
        weighted_avg = jnp.einsum('abhqk,abhkd->abhqd', weights, v)
        b1, b2, h, n, d = weighted_avg.shape
        weighted_avg = weighted_avg.transpose(0, 1, 3, 2, 4).reshape(b1, b2, n, h * d)
        gate = jax.nn.sigmoid(jnp.einsum('abnd,ed->abne', in_data, w_gate) + gating_bias)
        weighted_avg = gate * weighted_avg
        return jnp.einsum('abne,oe->abno', weighted_avg, w_o) + b_o

    def _gn(v, G=32, eps=1e-5):
        B_, H_, W_, C_ = v.shape
        g = v.reshape(B_, H_, W_, G, C_ // G)
        m = jnp.mean(g, axis=(1, 2, 4), keepdims=True)
        s = jnp.var(g, axis=(1, 2, 4), keepdims=True)
        return ((g - m) / jnp.sqrt(s + eps)).reshape(v.shape)

    def _ln_c(v, eps=1e-6):
        m = jnp.mean(v, axis=-1, keepdims=True)
        s = jnp.var(v, axis=-1, keepdims=True)
        return (v - m) / jnp.sqrt(s + eps)

    def _ln_t(v, eps=1e-5):
        m = jnp.mean(v, axis=-1, keepdims=True)
        s = jnp.var(v, axis=-1, keepdims=True)
        return (v - m) / jnp.sqrt(s + eps)

    def _to_tokens(v):
        B_, H_, W_, C_ = v.shape
        return v.reshape(B_, H_ * W_, C_)
    def _from_tokens(t, like):
        return t.reshape(like.shape)

    x = x + _L0_conv_ref(_gn(x), L0_conv_nonbatched_bias, L0_conv_Wq, L0_conv_Wk, L0_conv_Wv, L0_conv_Wg, L0_conv_gating_bias, L0_conv_Wo, L0_conv_bo)
    x = x + _L1_conv_ref(_gn(x), L1_conv_mask, L1_conv_nonbatched_bias, L1_conv_w_qkv, L1_conv_w_gate, L1_conv_gating_bias, L1_conv_w_o, L1_conv_b_o)
    return x


_drawn_inputs = setup_inputs


def setup_inputs(seed=0):
    import zlib

    import numpy as np

    out = dict(_drawn_inputs(seed))
    spreads = {'L0_conv_gating_bias': (1.0, 0.6),
     'L0_conv_bo': (0.0, 0.1),
     'L1_conv_gating_bias': (1.0, 0.6),
     'L1_conv_b_o': (0.0, 0.1)}
    factors = {'L0_conv_Wg': 26.385, 'L1_conv_w_gate': 23.533}
    for name, (base, spread) in spreads.items():
        noise = np.random.default_rng([zlib.crc32(name.encode()), seed]).standard_normal(out[name].shape)
        drawn = base * np.exp(spread * noise) if base else spread * noise
        out[name] = jnp.asarray(drawn.astype(out[name].dtype))
    for name, factor in factors.items():
        out[name] = (out[name] * factor).astype(out[name].dtype)
    return out
```

```python
import concourse.bass as bass
import concourse.mybir as mybir
from contextlib import ExitStack

ROWS, TOK, CH, HEADS, HC = 128, 256, 256, 8, 32
P = 128
CT = CH // P
TT = TOK // P
HG = HEADS // 4
GROUP = 8
W_SCALE = 256.0
SCALING = HC ** -0.5
COARSE = 2.0 ** 15
FINE = 8.0
MASK_ROW = 96
MAX_K = (96, 98)
EXP_K = 100
GN_EPS = 1e-5
GATE_CAP = 1e15
STAT_TOK = 2048
STAT_LOADS = ROWS * TOK // STAT_TOK
EXP_LAG = 4
UNROLL = 4
FIRST_LOOP, LAST_LOOP = 8, 124


def place(h):
    return h % 4 * HG + h // 4


class Row:

    def __init__(self, layer, turns, off):
        self.layer, self.turns, self.off = layer, turns, off

    def plus(self, n):
        return Row(self.layer, self.turns, self.off + n)

    def active(self):
        return not isinstance(self.turns, int) or 0 <= self.off < ROWS

    def index(self):
        return self.turns * UNROLL + self.off

    def ring(self, n):
        return self.off % n

    def count(self, per_row, c):
        return self.turns * (UNROLL * per_row) + ((self.off + self.layer * ROWS) * per_row + c)

    def lap(self, n, per_lap, c):
        return self.turns * (UNROLL // n * per_lap) + ((self.off + self.layer * ROWS) // n * per_lap + c)


def slots(engine, layer, body):
    for s in range(-2, FIRST_LOOP):
        body(Row(layer, 0, s))
    with engine.Fori(FIRST_LOOP // UNROLL, LAST_LOOP // UNROLL) as turns:
        for u in range(UNROLL):
            body(Row(layer, turns, u))
    for s in range(LAST_LOOP, ROWS + 6):
        body(Row(layer, 0, s))


def wait(engine, sem, value, passed=None):
    if isinstance(value, int) and value <= 0:
        return
    engine.wait_ge(sem, value)
    if passed is not None and not isinstance(value, int):
        engine.sem_inc(passed, 1)


def build(nc, a, out):
    f32, f16 = mybir.dt.float32, mybir.dt.float16
    ALU, ACT = mybir.AluOpType, mybir.ActivationFunctionType

    x1 = nc.dram_tensor("layer0_out", (CH, ROWS * TOK), f32, kind="Internal").ap()
    mask_dram = nc.dram_tensor("mask_pieces", (ROWS, 2, TOK), f16, kind="Internal").ap()
    src = [a["xT"], x1]
    dst = [x1, out]

    ctx = ExitStack()
    with ctx:
        def sb(name, shape, dt):
            return ctx.enter_context(nc.sbuf_tensor(name, shape, dt))

        def sem(name):
            return ctx.enter_context(nc.semaphore(name))

        bias_q = sb("bias_q", [P, HEADS, TT, TOK], f32)
        bias_k = sb("bias_k", [P, HEADS, TT, TOK], f32)
        w_hi = [[sb(f"w_hi{l}{m}", [P, CT, CH], f16) for m in "qkvg"] for l in range(2)]
        w_lo = [[sb(f"w_lo{l}{m}", [P, CT, CH], f16) for m in "qkvg"] for l in range(2)]
        w_out = [sb(f"w_out{l}", [P, CT, CH], f32) for l in range(2)]
        out_bias = sb("out_bias", [P, 2, CT], f32)
        gate_bias = sb("gate_bias", [P, 2, CT], f32)
        neg_gate_bias = sb("neg_gate_bias", [P, 2, CT], f32)
        group_avg = sb("group_avg", [P, P], f32)
        ident = sb("ident", [P, P], f16)
        ones = sb("ones", [P, HC], f32)
        mask_bias = sb("mask_bias", [P, ROWS, TT], f32)
        mask_row = sb("mask_row", [P, TOK], f32)
        mask_pc = sb("mask_pc", [P, 2, TOK], f16)
        stats = sb("stats", [P, CT, ROWS, 6], f32)
        mean_var = sb("mean_var", [P, CT, 2], f32)
        centred = sb("centred", [P, CT], f32)
        spread = sb("spread", [P, CT], f32)
        neg_mean = sb("neg_mean", [P, CT], f32)
        std = sb("std", [P, CT], f32)
        rstd = sb("rstd", [P, CT], f32)
        shift_x = sb("shift_x", [P, CT], f32)

        x_in = sb("x_in", [P, 2, CT, TOK], f32)
        x_norm = sb("x_norm", [P, 2, CT, TOK], f32)
        x_hi = sb("x_hi", [P, 2, CT, TOK], f16)
        x_lo = sb("x_lo", [P, 2, CT, TOK], f16)
        qk_f32 = [sb(f"{m}_f32", [P, 2, HG, TOK], f32) for m in "qk"]
        qk_hi = [sb(f"{m}_hi", [P, 2, HG, TOK], f16) for m in "qk"]
        qk_lo = [sb(f"{m}_lo", [P, 2, HG, TOK], f16) for m in "qk"]
        stack = [sb(f"{m}_stack", [P, 4, HEADS, TOK], f16) for m in "qk"]
        v_sb = sb("v_sb", [P, 4, TT, CH], f32)
        gate_exp = sb("gate_exp", [P, 4, HG, TOK], f32)
        row_max = sb("row_max", [P, 2, TT, HEADS], f32)
        max_pc = sb("max_pc", [P, 2, TT, 4, HEADS], f16)
        shift = sb("shift", [4 * HEADS, 2, TT, P], f16)
        probs = sb("probs", [P, 2, HEADS, TT, TOK], f32)
        probs_sum = sb("probs_sum", [P, HG, 4, TOK], f32)
        denom = sb("denom", [P, 2, HG, TOK], f32)
        log_den = sb("log_den", [P, HG, TOK], f32)
        recip = sb("recip", [P, HG, TOK], f32)
        newton = sb("newton", [P, HG, TOK], f32)
        recip_neg = sb("recip_neg", [P, HG, TOK], f32)
        gated = sb("gated", [P, 2, HG, TOK], f32)
        attn = sb("attn", [P, 2, CT, TOK], f32)
        y = sb("y", [P, 2, CT, TOK], f32)

        w_stage = probs[:, 0].rearrange("p h t k -> p (h t k)").rearrange(
            "p (l m c e) -> p l m c e", l=2, m=4, c=CT)
        x_stat = [t.rearrange("p h t k -> p (h t k)").rearrange("p (c t) -> p c t", c=CT)
                  for t in (probs[:, 1], bias_k[:, :, :, :])]

        def bank(name):
            return ctx.enter_context(nc.psum_tensor(name, [P, 2, TOK], f32))

        max_bank = [bank(f"max_bank{i}") for i in range(2)]
        exp_bank = [bank(f"exp_bank{i}") for i in range(2)]
        pa, pb = bank("proj_a"), bank("proj_b")
        av_bank, den_bank = bank("av_bank"), bank("den_bank")
        shift_ps = pb[:, :, :].rearrange("p a t -> p (a t)").bitcast(f16)

        sp_passed, pool_passed, act_passed, dve_passed = (sem(f"{e}_passed") for e in ("sp", "pool", "act", "dve"))
        const_in, w_in, bias_in, mask_in = sem("const_in"), sem("w_in"), sem("bias_in"), sem("mask_in")
        w_in1 = sem("w_in1")
        stack_init, mask_out = sem("stack_init"), sem("mask_out")
        stat_in = [sem(f"stat_in{i}") for i in range(2)]
        stat_used, w_hi_ready, w_lo_ready = sem("stat_used"), sem("w_hi_ready"), sem("w_lo_ready")
        zeroed, mask_bias_ready, gate_bias_ready = sem("zeroed"), sem("mask_bias_ready"), sem("gate_bias_ready")
        mask_step = sem("mask_step")
        norm_v, norm_c, norm_avg, norm_std = sem("norm_v"), sem("norm_c"), sem("norm_avg"), sem("norm_std")
        x_loaded = [sem(f"x_loaded{i}") for i in range(2)]
        x_norm_ready, x_hi_ready, x_lo_ready = sem("x_norm_ready"), sem("x_hi_ready"), sem("x_lo_ready")
        q_psum, k_psum, g_psum, v_psum = sem("q_psum"), sem("k_psum"), sem("g_psum"), sem("v_psum")
        qk_psum = [q_psum, k_psum]
        qk_hi_ready = [sem("q_hi_ready"), sem("k_hi_ready")]
        qk_f32_ready = [sem("q_f32_ready"), sem("k_f32_ready")]
        qk_lo_ready = [sem("q_lo_ready"), sem("k_lo_ready")]
        stack_in = [sem(f"stack_in{i}") for i in range(4)]
        STACK_INC = [6 * 16, 8 * 16]
        v_ready, gate_ready, gate_capped = sem("v_ready"), sem("gate_ready"), sem("gate_capped")
        max_psum, max_done = sem("max_psum"), sem("max_done")
        coarse_ready, fine_ready = sem("coarse_ready"), sem("fine_ready")
        shift_psum, shift_ready = sem("shift_psum"), sem("shift_ready")
        shift_in = [sem(f"shift_in{i}") for i in range(4)]
        exp_psum, logits_ready = sem("exp_psum"), sem("logits_ready")
        probs_ready, sum_ready = sem("probs_ready"), sem("sum_ready")
        av_psum, den_psum = sem("av_psum"), sem("den_psum")
        denom_ready, log_ready, recip_ready = sem("denom_ready"), sem("log_ready"), sem("recip_ready")
        newton_ready, recip_neg_ready = sem("newton_ready"), sem("recip_neg_ready")
        gated_ready, out_psum = sem("gated_ready"), sem("out_psum")
        res_in = [sem(f"res_in{i}") for i in range(2)]
        out_left = sem("out_left")
        y_ready, stats_ready = sem("y_ready"), sem("stats_ready")
        y_out = [sem(f"y_out{i}") for i in range(2)]

        def stack_full(r):
            inc = STACK_INC[r.layer]
            if not r.active():
                return 0
            return r.turns * inc + (r.off // 4 * inc + r.layer * (ROWS // 4) * STACK_INC[0] + inc)

        def channel_major(x, first, n):
            return x.rearrange("(c p) t -> p c t", p=P)[:, :, bass.ds(first, n)]

        block = ctx.enter_context(nc.Block())

        @block.sync
        def _(sp):
            sp.dma_start(group_avg[:, :], a["group_avg"]).then_inc(const_in, 16)
            sp.dma_start(ident[:, :], a["ident"]).then_inc(const_in, 16)
            for i, n in enumerate(("L0_conv_gating_bias", "L1_conv_gating_bias")):
                sp.dma_start(gate_bias[:, i, :], a[n], ).then_inc(const_in, 16)
            for i, n in enumerate(("L0_conv_bo", "L1_conv_b_o")):
                sp.dma_start(out_bias[:, i, :], a[n]).then_inc(const_in, 16)
            for l in range(2):
                for m in range(4):
                    sp.dma_start(w_stage[:, l, m], a["w_proj"][l, m].rearrange("(c p) e -> p c e", p=P)
                                 ).then_inc(w_in, 16)
                sp.dma_start(w_out[l][:, :, :], a["w_out"][l].rearrange("(c p) e -> p c e", p=P)).then_inc(w_in1, 16)
            for i in range(2):
                sp.dma_start(x_stat[i], channel_major(a["xT"], i * STAT_TOK, STAT_TOK)).then_inc(stat_in[i], 16)
            with sp.Fori(1, STAT_LOADS // 2) as c:
                for i in range(2):
                    wait(sp, stat_used, 2 * c + (i - 1), sp_passed)
                    sp.dma_start(x_stat[i], channel_major(a["xT"], c * (2 * STAT_TOK) + i * STAT_TOK, STAT_TOK)
                                 ).then_inc(stat_in[i], 16)
            sp.dma_start(mask_row[:, :], a["mask"]).then_inc(mask_in, 16)
            sp.dma_start(mask_bias[:, :, :], a["mask_k"]).then_inc(mask_in, 16)
            sp.wait_ge(zeroed, 4)
            for i in range(4):
                sp.dma_start(stack[1][MASK_ROW:MASK_ROW + 4, i], a["k_rows"]).then_inc(stack_init, 16)
            sp.wait_ge(mask_step, 3)
            sp.dma_start(mask_dram.rearrange("b r t -> b (r t)"), mask_pc[:, :, :].rearrange("p r t -> p (r t)")
                         ).then_inc(mask_out, 16)
            sp.wait_ge(mask_out, 16)
            sp.wait_ge(stack_init, 64)

            def load_bias(l):
                if l == 0:
                    sp.wait_ge(stat_used, STAT_LOADS)
                else:
                    sp.wait_ge(max_done, 8 * ROWS)
                    sp.wait_ge(logits_ready, 8 * ROWS)
                sp.dma_start(bias_q[:, :, :, :], a["bias_q"][l]).then_inc(bias_in, 16)
                sp.dma_start(bias_k[:, :, :, :], a["bias_k"][l]).then_inc(bias_in, 16)

            def slot(s):
                l = s.layer
                r = s.plus(2)
                if r.active():
                    i = r.ring(2)
                    wait(sp, x_norm_ready, r.plus(-2).count(1, 1), sp_passed)
                    sp.dma_start(x_in[:, i], channel_major(src[l], r.index() * TOK, TOK)).then_inc(x_loaded[i], 16)
                r = s.plus(-2)
                if r.active():
                    i = r.ring(4)
                    wait(sp, shift_ready, r.count(1, 1), sp_passed)
                    sp.dma_start(stack[0][MASK_ROW:MASK_ROW + 4, i],
                                 shift[:, r.ring(2)].rearrange("h t q -> h (t q)")).then_inc(shift_in[i], 16)
                r = s
                if r.active():
                    i, b = r.ring(4), r.ring(2)
                    wait(sp, exp_psum, r.plus(-4).count(8, 8), sp_passed)
                    if l == 1:
                        sp.dma_start(stack[0][MASK_ROW:MASK_ROW + 2, i], a["q_rows"]).then_inc(stack_in[i], 16)
                        sp.dma_start(stack[1][MASK_ROW:MASK_ROW + 2, i],
                                     mask_dram[bass.ds(r.index(), 1)].rearrange("o r t -> (o r) t")
                                     .unsqueeze(1).broadcast_to([2, HEADS, TOK])).then_inc(stack_in[i], 16)
                    for m in range(2):
                        his = (0, 1) if m == 0 else (0, 2)
                        lo = 2 if m == 0 else 1
                        for part, ready, where in ((qk_hi, qk_hi_ready, his), (qk_lo, qk_lo_ready, (lo,))):
                            wait(sp, ready[m], r.count(1, 1), sp_passed)
                            for w in where:
                                sp.dma_start(stack[m][HC * w:HC * (w + 1), i], part[m][:, b]).then_inc(stack_in[i], 16)
                r = s.plus(-5)
                if r.active():
                    i = r.ring(2)
                    wait(sp, y_ready, r.count(1, 1), sp_passed)
                    sp.dma_start(channel_major(dst[l], r.index() * TOK, TOK), y[:, i]).then_inc(y_out[i], 16)
                r = s.plus(-4)
                if r.active():
                    i = r.ring(2)
                    wait(sp, y_out[i], r.plus(-2).lap(2, 16, 16), sp_passed)
                    if l == 0:
                        wait(sp, stats_ready, r.plus(-2).count(1, 1), sp_passed)
                    sp.dma_start(y[:, i], channel_major(src[l], r.index() * TOK, TOK)).then_inc(res_in[i], 16)

            for l in range(2):
                load_bias(l)
                if l:
                    for i in range(2):
                        sp.wait_ge(y_out[i], 16 * (ROWS // 2))
                    sp.wait_ge(stats_ready, ROWS)
                slots(sp, l, slot)
            for i in range(2):
                sp.wait_ge(y_out[i], 16 * ROWS)

        @block.gpsimd
        def _(pool):
            pool.memset(ones[:, :], 1.0).then_inc(zeroed, 1)
            for m in range(2):
                pool.wait_ge(zeroed, m + 1)
                pool.memset(stack[m][MASK_ROW:P, :, :, :], 0.0).then_inc(zeroed, 1)
            pool.wait_ge(zeroed, 3)
            pool.memset(max_pc[:, :, :, :, :], 0.0).then_inc(zeroed, 1)
            pool.wait_ge(const_in, 96)
            pool.tensor_scalar(neg_gate_bias[:, :, :], gate_bias[:, :, :], -1.0, 1.0, ALU.mult, ALU.mult
                               ).then_inc(gate_bias_ready, 1)

            def slot(s):
                l = s.layer
                r = s.plus(-3)
                if r.active():
                    key_sum(r, 0)
                r = s.plus(-4)
                if r.active():
                    wait(pool, recip_neg_ready, r.plus(-1).count(1, 1))
                    wait(pool, denom_ready, r.count(1, 1))
                    wait(pool, recip_ready, r.count(1, 1), pool_passed)
                    pool.tensor_tensor(newton[:, :, :], denom[:, r.ring(2)], recip[:, :, :], ALU.mult
                                       ).then_inc(newton_ready, 1)
                r = s.plus(-5)
                if r.active():
                    i = r.ring(2)
                    wait(pool, res_in[i], r.lap(2, 16, 16))
                    wait(pool, out_left, r.count(1, 1), pool_passed)
                    pool.tensor_tensor(y[:, i], y[:, i], attn[:, i], ALU.add).then_inc(y_ready, 1)
                if s.active():
                    low_half(s, 0)
                if s.active():
                    low_half(s, 1)
                r = s.plus(-3)
                if r.active():
                    key_sum(r, 1)
                r = s.plus(-1)
                if r.active():
                    wait(pool, gate_ready, r.count(1, 1), pool_passed)
                    g = gate_exp[:, r.ring(4)]
                    pool.tensor_scalar(g, g, GATE_CAP, 0.0, ALU.min, ALU.max).then_inc(gate_capped, 1)
                r = s.plus(1)
                if r.active():
                    i = r.ring(2)
                    wait(pool, x_norm_ready, r.count(1, 1))
                    wait(pool, g_psum, r.plus(-2).count(1, 1))
                    wait(pool, x_hi_ready, r.count(1, 1), pool_passed)
                    pool.tensor_tensor(x_lo[:, i], x_norm[:, i], x_hi[:, i], ALU.subtract).then_inc(x_lo_ready, 1)

            def low_half(r, m):
                b = r.ring(2)
                wait(pool, qk_f32_ready[m], r.count(1, 1), pool_passed)
                wait(pool, qk_hi_ready[m], r.count(1, 1), pool_passed)
                q = r.plus(-2)
                wait(pool, stack_in[q.ring(4)], stack_full(q), pool_passed)
                pool.tensor_tensor(qk_lo[m][:, b], qk_f32[m][:, b], qk_hi[m][:, b], ALU.subtract
                                   ).then_inc(qk_lo_ready[m], 1)

            def key_sum(r, g):
                wait(pool, probs_ready, r.count(4, 2 * g + 2), pool_passed)
                wait(pool, den_psum, r.plus(-1).count(2, g + 1), pool_passed)
                pr = probs[:, r.ring(2), 4 * g:4 * (g + 1)]
                pool.tensor_tensor(probs_sum[:, g], pr[:, :, 0, :], pr[:, :, 1, :], ALU.add).then_inc(sum_ready, 1)

            for l in range(2):
                slots(pool, l, slot)

        @block.scalar
        def _(act):
            act.wait_ge(w_in, 16 * 8)
            for l in range(2):
                for m in range(4):
                    act.activation(w_hi[l][m][:, :, :], w_stage[:, l, m], ACT.Copy, scale=W_SCALE
                                   ).then_inc(w_hi_ready, 1)

            def exponentials(r, g):
                l, i = r.layer, r.ring(2)
                wait(act, logits_ready, r.count(8, 4 * g + 4), act_passed)
                for t in range(TT):
                    pr = probs[:, i, 4 * g:4 * (g + 1), t, :]
                    if l:
                        act.activation(pr, pr, ACT.Exp, bias=mask_bias[:, bass.ds(r.index(), 1), t]
                                       ).then_inc(probs_ready, 1)
                    else:
                        act.activation(pr, pr, ACT.Exp).then_inc(probs_ready, 1)

            def split(r, m):
                b = r.ring(2)
                ps = (pa, pb)[m]
                scale = (SCALING if m == 0 else 1.0) / W_SCALE
                act.wait_ge(qk_psum[m], r.count(1, 1))
                q = r.plus(-2)
                wait(act, stack_in[q.ring(4)], stack_full(q))
                wait(act, qk_lo_ready[m], r.plus(-2).count(1, 1))
                act.activation(qk_hi[m][:, b], ps[:, :, :], ACT.Copy, scale=scale).then_inc(qk_hi_ready[m], 1)
                act.activation(qk_f32[m][:, b], ps[:, :, :], ACT.Copy, scale=scale).then_inc(qk_f32_ready[m], 1)

            def slot(s):
                l = s.layer
                r = s.plus(-2)
                if r.active():
                    i = r.ring(2)
                    act.wait_ge(shift_psum, r.count(1, 1))
                    q = r.plus(-2)
                    wait(act, shift_in[q.ring(4)], q.lap(4, 16, 16))
                    act.activation(shift[:, i].rearrange("h t q -> h (t q)"), shift_ps[0:4 * HEADS, 0:TOK], ACT.Copy
                                   ).then_inc(shift_ready, 1)
                r = s.plus(-4)
                if r.active():
                    act.wait_ge(denom_ready, r.count(1, 1))
                    act.activation(log_den[:, :, :], denom[:, r.ring(2)], ACT.Ln).then_inc(log_ready, 1)
                r = s.plus(-4)
                if r.active():
                    act.wait_ge(log_ready, r.count(1, 1))
                    wait(act, recip_neg_ready, r.plus(-1).count(1, 1))
                    act.activation(recip[:, :, :], log_den[:, :, :], ACT.Exp, scale=-1.0).then_inc(recip_ready, 1)
                if s.active():
                    split(s, 0)
                if s.active():
                    split(s, 1)
                r = s.plus(-3)
                if r.active():
                    exponentials(r, 1)
                if s.active():
                    act.wait_ge(v_psum, s.count(1, 1))
                    wait(act, av_psum, s.plus(-4).count(2, 2))
                    act.activation(v_sb[:, s.ring(4)], pa[:, :, :], ACT.Copy, scale=1.0 / W_SCALE).then_inc(v_ready, 1)
                r = s.plus(1)
                if r.active():
                    i = r.ring(2)
                    if r.off == 0 and isinstance(r.turns, int):
                        act.wait_ge(norm_v, 6 * (l + 1))
                    wait(act, x_lo_ready, r.plus(-2).count(1, 1))
                    act.wait_ge(x_loaded[i], r.lap(2, 16, 16))
                    for c in range(CT):
                        op = act.activation(x_norm[:, i, c], x_in[:, i, c], ACT.Identity,
                                            bias=shift_x[:, c:c + 1], scale=rstd[:, c:c + 1])
                    op.then_inc(x_norm_ready, 1)
                    act.wait_ge(x_norm_ready, r.count(1, 1))
                    wait(act, g_psum, r.plus(-2).count(1, 1))
                    act.activation(x_hi[:, i], x_norm[:, i], ACT.Copy).then_inc(x_hi_ready, 1)
                if s.active():
                    if s.off == 0 and isinstance(s.turns, int) and l == 0:
                        act.wait_ge(gate_bias_ready, 1)
                    act.wait_ge(g_psum, s.count(1, 1))
                    wait(act, denom_ready, s.plus(-4).count(1, 1))
                    for g in range(HG):
                        op = act.activation(gate_exp[:, s.ring(4), g], pb[:, g, :], ACT.Exp,
                                            bias=neg_gate_bias[:, l, g:g + 1], scale=-1.0 / W_SCALE)
                    op.then_inc(gate_ready, 1)
                r = s.plus(-4)
                if r.active():
                    i = r.ring(2)
                    act.wait_ge(out_psum, r.count(1, 1))
                    wait(act, y_ready, r.plus(-2).count(1, 1))
                    for c in range(CT):
                        op = act.activation(attn[:, i, c], pa[:, c, :], ACT.Identity, bias=out_bias[:, l, c:c + 1])
                    op.then_inc(out_left, 1)
                r = s.plus(-2)
                if r.active():
                    exponentials(r, 0)

            for l in range(2):
                act.wait_ge(norm_avg, 2 * l + 2)
                act.wait_ge(norm_v, 6 * l + 4)
                act.activation(std[:, :], spread[:, :], ACT.Sqrt).then_inc(norm_std, 1)
                act.preload_act_table_set("natural_log_exp_and_others")
                slots(act, l, slot)

        @block.vector
        def _(dve):
            for l in range(2):
                for m in range(4):
                    dve.wait_ge(w_hi_ready, 4 * l + m + 1)
                    dve.scalar_tensor_tensor(out=w_lo[l][m][:, :, :], in0=w_stage[:, l, m], scalar=W_SCALE,
                                             in1=w_hi[l][m][:, :, :], op0=ALU.mult, op1=ALU.subtract
                                             ).then_inc(w_lo_ready, 1)
            n = STAT_TOK // 512
            with dve.Fori(0, STAT_LOADS // 2) as c:
                for i in range(2):
                    dve.wait_ge(stat_in[i], c * 16 + 16)
                    for ct in range(CT):
                        for t in range(n):
                            op = dve.bn_stats(stats[:, ct, bass.ds(c * (2 * n) + (i * n + t), 1), :],
                                              x_stat[i][:, ct, t * 512:(t + 1) * 512])
                    op.then_inc(stat_used, 1)
            dve.wait_ge(mask_in, 32)
            for t in (mask_bias[:, :, :], mask_row[:, :]):
                op = dve.tensor_scalar(t, t, -1.0, 1e9, ALU.add, ALU.mult)
            op.then_inc(mask_step, 1)
            dve.wait_ge(mask_step, 1)
            dve.tensor_scalar(mask_pc[:, 0, :], mask_row[:, :], 1.0 / COARSE, None, ALU.mult).then_inc(mask_step, 1)
            dve.wait_ge(mask_step, 2)
            fine = mask_row
            dve.scalar_tensor_tensor(out=fine[:, :], in0=mask_pc[:, 0, :], scalar=-COARSE, in1=mask_row[:, :],
                                     op0=ALU.mult, op1=ALU.add).then_inc(mask_bias_ready, 1)
            dve.wait_ge(mask_bias_ready, 1)
            dve.tensor_scalar(mask_pc[:, 1, :], fine[:, :], 1.0 / FINE, None, ALU.mult).then_inc(mask_step, 1)

            def normalisation(l):
                chunks = ROWS if l else ROWS * TOK // 512
                if l:
                    dve.wait_ge(stats_ready, ROWS)
                else:
                    dve.wait_ge(stat_used, STAT_LOADS)
                for c in range(CT):
                    op = dve.bn_aggr(mean_var[:, c, :], stats[:, c, 0:chunks, :].rearrange("p a b -> p (a b)"))
                op.then_inc(norm_v, 1)
                dve.wait_ge(norm_avg, 2 * l + 1)
                dve.tensor_tensor(centred[:, :], pa[:, 0, 0:CT], mean_var[:, :, 0], ALU.subtract).then_inc(norm_v, 1)
                dve.tensor_scalar(neg_mean[:, :], pa[:, 0, 0:CT], -1.0, None, ALU.mult)
                dve.wait_ge(norm_v, 6 * l + 2)
                dve.tensor_tensor(centred[:, :], centred[:, :], centred[:, :], ALU.mult).then_inc(norm_v, 1)
                dve.wait_ge(norm_v, 6 * l + 3)
                dve.tensor_tensor(mean_var[:, :, 1], mean_var[:, :, 1], centred[:, :], ALU.add).then_inc(norm_c, 1)
                dve.wait_ge(norm_avg, 2 * l + 2)
                dve.tensor_scalar(spread[:, :], pb[:, 0, 0:CT], GN_EPS, None, ALU.add).then_inc(norm_v, 1)
                dve.wait_ge(norm_std, l + 1)
                dve.reciprocal(rstd[:, :], std[:, :]).then_inc(norm_v, 1)
                dve.wait_ge(norm_v, 6 * l + 5)
                dve.tensor_tensor(shift_x[:, :], neg_mean[:, :], rstd[:, :], ALU.mult).then_inc(norm_v, 1)

            def maxima(r, h):
                i = r.ring(2)
                if h == 0:
                    wait(dve, fine_ready, r.plus(-2).count(1, 1))
                wait(dve, max_psum, r.count(8, h + 1), dve_passed)
                for t in range(TT):
                    op = dve.tensor_tensor_reduce(out=max_bank[h % 2][:, t, :], in0=max_bank[h % 2][:, t, :],
                                                  in1=bias_q[:, h, t, :], scale=1.0 / FINE, scalar=-3.0e38,
                                                  op0=ALU.add, op1=ALU.max, accum_out=row_max[:, i, t, place(h):place(h) + 1])
                op.then_inc(max_done, 1)

            def logits(r, h):
                dve.wait_ge(exp_psum, r.count(8, h + 1))
                if h % 4 == 0:
                    wait(dve, av_psum, r.plus(-2).count(2, h // 4 + 1))
                    wait(dve, sum_ready, r.plus(-2).count(2, h // 4 + 1))
                dve.tensor_tensor(probs[:, r.ring(2), h], exp_bank[h % 2][:, :, :], bias_k[:, h], ALU.add
                                  ).then_inc(logits_ready, 1)

            def slot(s):
                l = s.layer
                for step in range(8):
                    r = s.plus(-1)
                    if r.active():
                        maxima(r, step)
                    h = (step + EXP_LAG) % 8
                    r = s.plus(-3 if step < 8 - EXP_LAG else -2)
                    if r.active():
                        logits(r, h)
                    r = s.plus(-1)
                    if step == 7 and r.active():
                        i = r.ring(2)
                        dve.wait_ge(max_done, r.count(8, 8))
                        wait(dve, shift_psum, r.plus(-2).count(1, 1))
                        dve.tensor_scalar(max_pc[:, i, :, 2, :], row_max[:, i], -FINE / COARSE, None, ALU.mult
                                          ).then_inc(coarse_ready, 1)
                        dve.wait_ge(coarse_ready, r.count(1, 1))
                        dve.scalar_tensor_tensor(out=max_pc[:, i, :, 3, :], in0=max_pc[:, i, :, 2, :], scalar=COARSE / FINE, in1=row_max[:, i],
                                                 op0=ALU.mult, op1=ALU.add).then_inc(fine_ready, 1)
                    r = s.plus(-5)
                    if step == 6 and l == 0 and r.active():
                        dve.wait_ge(y_ready, r.count(1, 1))
                        for c in range(CT):
                            op = dve.bn_stats(stats[:, c, bass.ds(r.index(), 1), :], y[:, r.ring(2), c])
                        op.then_inc(stats_ready, 1)
                    r = s.plus(-4)
                    if step == 1 and r.active():
                        i = r.ring(2)
                        dve.wait_ge(den_psum, r.count(2, 2))
                        dve.wait_ge(gate_capped, r.count(1, 1))
                        wait(dve, newton_ready, r.plus(-2).count(1, 1))
                        wait(dve, log_ready, r.plus(-2).count(1, 1))
                        dve.scalar_tensor_tensor(out=denom[:, i], in0=gate_exp[:, r.ring(4)], scalar=1.0,
                                                 in1=den_bank[:, :, :], op0=ALU.add, op1=ALU.mult
                                                 ).then_inc(denom_ready, 1)
                    if step == 4 and r.active():
                        i = r.ring(2)
                        dve.wait_ge(newton_ready, r.count(1, 1))
                        dve.scalar_tensor_tensor(out=recip_neg[:, :, :], in0=newton[:, :, :], scalar=-2.0,
                                                 in1=recip[:, :, :], op0=ALU.add, op1=ALU.mult
                                                 ).then_inc(recip_neg_ready, 1)
                        dve.wait_ge(recip_neg_ready, r.count(1, 1))
                        dve.wait_ge(av_psum, r.count(2, 2))
                        wait(dve, out_psum, r.plus(-2).count(1, 1))
                        dve.scalar_tensor_tensor(out=gated[:, i], in0=av_bank[:, :, :], scalar=-1.0,
                                                 in1=recip_neg[:, :, :], op0=ALU.mult, op1=ALU.mult
                                                 ).then_inc(gated_ready, 1)

            for l in range(2):
                normalisation(l)
                dve.wait_ge(bias_in, 32 * (l + 1))
                slots(dve, l, slot)

        @block.tensor
        def _(pe):
            pe.wait_ge(const_in, 96)
            pe.wait_ge(zeroed, 4)
            pe.wait_ge(w_lo_ready, 8)
            pe.wait_ge(w_in1, 32)

            def project(r, m, ps, tile, last):
                l, b = r.layer, r.ring(2)
                terms = [(w, x, c) for w, x in ((w_hi, x_hi), (w_lo, x_hi), (w_hi, x_lo)) for c in range(CT)]
                cut = slice(tile * P, (tile + 1) * P)
                for n, (w, x, c) in enumerate(terms):
                    if m == 2:
                        lhs, rhs = x[:, b, c, cut], w[l][m][:, c, :]
                    else:
                        lhs, rhs = w[l][m][:, c, cut], x[:, b, c, :]
                    op = pe.matmul(ps[:, tile, :], lhs, rhs, start=(n == 0), stop=(n == len(terms) - 1))
                if last is not None:
                    op.then_inc(last, 1)

            def logits(r, h, of_max):
                i = r.ring(4)
                q, k = stack[0][:, i, place(h)], stack[1][:, i, place(h)]
                if of_max:
                    wait(pe, max_done, r.count(8, h - 1))
                    n, bank_, done = MAX_K[r.layer], max_bank[h % 2], max_psum
                    for t in range(TT):
                        op = pe.matmul(bank_[:, t, :], q[0:n, t * P:(t + 1) * P], k[0:n, :], start=True, stop=True)
                else:
                    wait(pe, logits_ready, r.count(8, h - 1))
                    n, bank_, done = EXP_K, exp_bank[h % 2], exp_psum
                    for t in range(TT):
                        op = pe.matmul(bank_[:, t, :], k[0:n, t * P:(t + 1) * P], q[0:n, :], start=True, stop=True)
                op.then_inc(done, 1)

            def average(r, g):
                pe.wait_ge(probs_ready, r.count(4, 2 * g + 2))
                pe.wait_ge(v_ready, r.count(1, 1))
                if g == 0:
                    wait(pe, gated_ready, r.plus(-1).count(1, 1))
                for t in range(TT):
                    for j in range(4):
                        h = 4 * g + j
                        op = pe.matmul(av_bank[HC * j:HC * (j + 1), g, :], v_sb[:, r.ring(4), t, HC * h:HC * (h + 1)],
                                       probs[:, r.ring(2), h, t, :], start=(t == 0), stop=(t == TT - 1))
                op.then_inc(av_psum, 1)

            def denominator(r, g):
                pe.wait_ge(sum_ready, r.count(2, g + 1))
                if g == 0:
                    wait(pe, denom_ready, r.plus(-1).count(1, 1))
                for j in range(4):
                    op = pe.matmul(den_bank[HC * j:HC * (j + 1), g, :], ones[:, :], probs_sum[:, g, j, :],
                                   start=True, stop=True)
                op.then_inc(den_psum, 1)

            def maxima_rows(r):
                pe.wait_ge(fine_ready, r.count(1, 1))
                if r.plus(1).active():
                    pe.wait_ge(gate_ready, r.plus(1).count(1, 1))
                wait(pe, shift_ready, r.plus(-1).count(1, 1))
                i = r.ring(2)
                for t in range(TT):
                    op = pe.transpose(shift_ps[0:4 * HEADS, t * P:(t + 1) * P],
                                      max_pc[:, i, t].rearrange("p a h -> p (a h)"), ident[:, :])
                op.then_inc(shift_psum, 1)

            def output(r):
                l, b = r.layer, r.ring(2)
                pe.wait_ge(gated_ready, r.count(1, 1))
                for o in range(CT):
                    for e in range(CT):
                        op = pe.matmul(pa[:, o, :], w_out[l][:, e, o * P:(o + 1) * P], gated[:, b, e, :],
                                       start=(e == 0), stop=(e == CT - 1))
                op.then_inc(out_psum, 1)

            def slot(s):
                for step in range(8):
                    r = s.plus(-1)
                    if r.active():
                        if step == 0:
                            i = r.ring(4)
                            pe.wait_ge(stack_in[i], stack_full(r))
                        logits(r, step, True)
                    h = (step + EXP_LAG) % 8
                    r = s.plus(-3 if step < 8 - EXP_LAG else -2)
                    if r.active():
                        if h == 0:
                            pe.wait_ge(shift_in[r.ring(4)], r.lap(4, 16, 16))
                        logits(r, h, False)
                    if step == 0:
                        r = s.plus(-4)
                        if r.active():
                            average(r, 1)
                            denominator(r, 1)
                    if step == 1:
                        r = s.plus(-2)
                        if r.active():
                            maxima_rows(r)
                        if s.active():
                            wait(pe, out_left, s.plus(-5).count(1, 1))
                            wait(pe, v_ready, s.plus(-1).count(1, 1))
                            pe.wait_ge(x_hi_ready, s.count(1, 1))
                            pe.wait_ge(x_lo_ready, s.count(1, 1))
                            project(s, 0, pa, 0, None)
                    if step == 2 and s.active():
                        project(s, 0, pa, 1, q_psum)
                    if step == 3:
                        if s.active():
                            wait(pe, gate_ready, s.plus(-1).count(1, 1))
                            wait(pe, shift_ready, s.plus(-2).count(1, 1))
                            project(s, 1, pb, 0, None)
                        r = s.plus(-3)
                        if r.active():
                            denominator(r, 0)
                    if step == 4 and s.active():
                        project(s, 1, pb, 1, k_psum)
                        pe.wait_ge(qk_f32_ready[0], s.count(1, 1))
                        project(s, 2, pa, 0, None)
                    if step == 5 and s.active():
                        project(s, 2, pa, 1, v_psum)
                        pe.wait_ge(qk_f32_ready[1], s.count(1, 1))
                        project(s, 3, pb, 0, None)
                    if step == 6:
                        if s.active():
                            project(s, 3, pb, 1, g_psum)
                        r = s.plus(-3)
                        if r.active():
                            average(r, 0)
                    if step == 7:
                        r = s.plus(-4)
                        if r.active():
                            if s.active():
                                pe.wait_ge(v_ready, s.count(1, 1))
                            else:
                                pe.wait_ge(v_ready, (s.layer + 1) * ROWS)
                                wait(pe, out_left, r.plus(-1).count(1, 1))
                            output(r)

            for l in range(2):
                pe.wait_ge(norm_v, 6 * l + 1)
                pe.matmul(pa[:, 0, 0:CT], group_avg[:, :], mean_var[:, :, 0], start=True, stop=True).then_inc(norm_avg, 1)
                pe.wait_ge(norm_c, l + 1)
                pe.matmul(pb[:, 0, 0:CT], group_avg[:, :], mean_var[:, :, 1], start=True, stop=True).then_inc(norm_avg, 1)
                slots(pe, l, slot)


def kernel(**inputs):
    import numpy as np
    import concourse.bacc as bacc
    from concourse.bass_utils import run_bass_kernel_spmd

    def get(name):
        return np.asarray(inputs[name])

    x = np.ascontiguousarray(get("x")[0].transpose(2, 0, 1).reshape(CH, ROWS * TOK))
    qkv = get("L1_conv_w_qkv").reshape(3, CH, CH)
    projections = [[get("L0_conv_Wq"), get("L0_conv_Wk"), get("L0_conv_Wv"), get("L0_conv_Wg")],
                   [qkv[0], qkv[1], qkv[2], get("L1_conv_w_gate")]]
    def by_channel(w):
        return w.T.reshape(CH, HG, 4, HC).transpose(0, 1, 3, 2).reshape(CH, CH)

    bias = np.stack([get("L0_conv_nonbatched_bias")[0], get("L1_conv_nonbatched_bias")[0]])
    mask = get("L1_conv_mask")[0]
    stack_rows = np.zeros((4, HEADS, TOK), np.float16)
    stack_rows[2], stack_rows[3] = COARSE, -FINE
    mask_rows = np.zeros((2, HEADS, TOK), np.float16)
    mask_rows[0], mask_rows[1] = COARSE, FINE
    arrays = {
        "xT": x,
        "w_proj": np.stack([np.stack([by_channel(ws[0]), by_channel(ws[1]), ws[2].T, ws[3].T]) for ws in projections]),
        "w_out": np.stack([get("L0_conv_Wo").T, get("L1_conv_w_o").T]),
        "bias_q": bias.reshape(2, HEADS, TT, P, TOK).transpose(0, 3, 1, 2, 4),
        "bias_k": bias.reshape(2, HEADS, TOK, TT, P).transpose(0, 4, 1, 3, 2),
        "mask": mask,
        "mask_k": mask.reshape(ROWS, TT, P).transpose(2, 0, 1),
        "group_avg": np.kron(np.eye(P // GROUP, dtype=np.float32), np.full((GROUP, GROUP), 1.0 / GROUP, np.float32)),
        "ident": np.eye(P, dtype=np.float16),
        "k_rows": stack_rows,
        "q_rows": mask_rows,
    }
    for name in ("L0_conv_gating_bias", "L1_conv_gating_bias", "L0_conv_bo", "L1_conv_b_o"):
        arrays[name] = get(name).reshape(CT, P).T
    arrays = {name: np.ascontiguousarray(v) for name, v in arrays.items()}
    nc = bacc.Bacc("TRN2", target_bir_lowering=False, num_devices=1)
    aps = {name: nc.dram_tensor("in_" + name, v.shape, mybir.dt.from_np(v.dtype), kind="ExternalInput").ap()
           for name, v in arrays.items()}
    out = nc.dram_tensor("out", (CH, ROWS * TOK), mybir.dt.float32, kind="ExternalOutput").ap()
    build(nc, aps, out)
    r = run_bass_kernel_spmd(nc, [{"in_" + name: v for name, v in arrays.items()}], core_ids=[0])
    return np.ascontiguousarray(r.results[0]["out"].reshape(CH, ROWS, TOK).transpose(1, 2, 0))[None]
```
